# Optimizing a Trainium2 kernel written in Bass

```python
import numpy as np
import jax
import jax.numpy as jnp

def _softmax(x, axis=-1):
    return jax.nn.softmax(x, axis=axis)

def _gelu(x):
    return jax.nn.gelu(x, approximate=True)

def _silu(x):
    return jax.nn.silu(x)

def _sigmoid(x):
    return jax.nn.sigmoid(x)

def _layernorm(x, axis=-1, eps=1e-05):
    m = jnp.mean(x, axis=axis, keepdims=True)
    v = jnp.var(x, axis=axis, keepdims=True)
    return (x - m) / jnp.sqrt(v + eps)

def _scatter_add(tgt, idx, src, axis=0):
    return tgt.at[idx].add(src)

def _segment_sum(src, seg, n):
    return jax.ops.segment_sum(src, seg, n)
kernel_name = 'mk_xattn_ffn_d2_seqx_r4_6aefb0'

def setup_inputs(seed: int=0):
    np.random.seed(seed)
    _w = jnp.asarray

    def _rec_inputs():
        import jax
        import jax.numpy as jnp
        _rk = jax.random.key(seed)
        x = -0.0002928 + 1 * jax.random.normal(jax.random.fold_in(_rk, 1), (8, 112, 256), jnp.float32)
        _lenS = 112 - jax.random.randint(jax.random.fold_in(_rk, 7), (8,), 0, max(1, 112 // 4) + 1, jnp.int32)
        _lenS2 = 375 - jax.random.randint(jax.random.fold_in(_rk, 8), (8,), 0, max(1, 375 // 4) + 1, jnp.int32)
        _ctx_1024P = jax.random.normal(jax.random.fold_in(_rk, 11), (8, 16, 256), jnp.float32)
        _ctx_1024c = jax.random.dirichlet(jax.random.fold_in(_rk, 511), 0.3 * jnp.ones((16,), jnp.float32), (8, 375))
        _ctx_1024t = jnp.einsum('bsk,bkd->bsd', _ctx_1024c, _ctx_1024P)
        _ctx_1024t = _ctx_1024t * jax.lax.rsqrt(jnp.mean(jnp.square(_ctx_1024t)) + 1e-12) * 0.953939
        ctx_1024 = -1.39393e-06 + 0.999914 * (_ctx_1024t + 0.3 * jax.random.normal(jax.random.fold_in(_rk, 611), (8, 375, 256), jnp.float32))
        _validS = jnp.arange(112)[None, :] < _lenS[:, None]
        _validS2 = jnp.arange(375)[None, :] < _lenS2[:, None]
        _causal = jnp.tril(jnp.ones((112, 112), dtype=bool))
        mask_SxS2_fk0 = jnp.where(jnp.broadcast_to(_validS2[0:1, :], (112, 375)), -1000000000.0, 0.0).astype(jnp.float32)
        return (x, ctx_1024, mask_SxS2_fk0)
    x, ctx_1024, mask_SxS2_fk0 = _rec_inputs()

    def _L0_xattn_setup():
        import jax, jax.numpy as jnp
        import numpy as np
        EMBED_DIM = 256
        NUM_HEADS = 16
        HEAD_DIM = EMBED_DIM // NUM_HEADS
        SCALE = HEAD_DIM ** (-0.5)
        key = jax.random.key(seed)
        ks = jax.random.split(key, 8)
        B, Nq, Nkv, C = (2, 512, 512, EMBED_DIM)
        s = C ** (-0.5)
        return {'q': jax.random.normal(ks[0], (B, Nq, C), dtype=jnp.float32), 'kv': jax.random.normal(ks[1], (B, Nkv, C), dtype=jnp.float32), 'w_q': jax.random.normal(ks[2], (C, C), dtype=jnp.float32) * s, 'b_q': jnp.zeros((C,), dtype=jnp.float32), 'w_kv': jax.random.normal(ks[3], (C, 2 * C), dtype=jnp.float32) * s, 'b_kv': jnp.zeros((2 * C,), dtype=jnp.float32), 'w_out': jax.random.normal(ks[4], (C, C), dtype=jnp.float32) * s, 'b_out': jnp.zeros((C,), dtype=jnp.float32)}
    _L0_xattn_all = _L0_xattn_setup()
    _L0_xattn_in = {k: v for k, v in _L0_xattn_all.items() if k in ('w_q', 'b_q', 'w_kv', 'b_kv', 'w_out', 'b_out')}
    del _L0_xattn_all

    def _L0_ffn_setup():
        import jax, jax.numpy as jnp
        import numpy as np
        import math
        MAX_NORM = 0.95
        CURVATURE = 1.0
        TOP_K = 2
        EPS = 1e-07

        def _project_to_ball(x):
            norm = jnp.clip(jnp.linalg.norm(x, axis=-1, keepdims=True), EPS, None)
            scale = jnp.where(norm > MAX_NORM, MAX_NORM / norm, jnp.ones_like(norm))
            return x * scale
        key = jax.random.key(seed)
        ks = jax.random.split(key, 8)
        B, N, D, E, F = (2, 512, 256, 8, 1024)
        x = jax.random.normal(ks[0], (B, N, D), dtype=jnp.float32)
        c = jax.random.normal(ks[1], (E, D), dtype=jnp.float32)
        centroids = c / jnp.linalg.norm(c, axis=-1, keepdims=True) * 0.5
        Wp = jax.random.normal(ks[2], (D, D), dtype=jnp.float32) * 0.02
        bp = jnp.zeros((D,), dtype=jnp.float32)
        W1 = jax.random.normal(ks[3], (E, D, F), dtype=jnp.float32) * 0.02
        b1 = jnp.zeros((E, F), dtype=jnp.float32)
        W2 = jax.random.normal(ks[4], (E, F, D), dtype=jnp.float32) * 0.02
        b2 = jnp.zeros((E, D), dtype=jnp.float32)
        return {'x': x, 'centroids': centroids, 'Wp': Wp, 'bp': bp, 'W1': W1, 'b1': b1, 'W2': W2, 'b2': b2}
    _L0_ffn_all = _L0_ffn_setup()
    _L0_ffn_in = {k: v for k, v in _L0_ffn_all.items() if k in ('centroids', 'Wp', 'bp', 'W1', 'b1', 'W2', 'b2')}
    del _L0_ffn_all

    def _L1_xattn_setup():
        import jax, jax.numpy as jnp
        import numpy as np
        B, S, D, H = (2, 512, 256, 16)
        A = D // H
        NEG = -1000000000.0
        key = jax.random.key(seed)
        ks = jax.random.split(key, 5)
        std = 1.0 / np.sqrt(D)
        query = jax.random.normal(ks[0], (B, S, D), dtype=jnp.float32)
        context = jax.random.normal(ks[1], (B, S, D), dtype=jnp.float32)
        Wq = jax.random.normal(ks[2], (D, D), dtype=jnp.float32) * std
        Wkv = jax.random.normal(ks[3], (2 * D, D), dtype=jnp.float32) * std
        Wout = jax.random.normal(ks[4], (D, D), dtype=jnp.float32) * std
        mask = jnp.where(jnp.tril(jnp.ones((S, S), dtype=bool)), 0.0, NEG).astype(jnp.float32)
        return {'query': query, 'context': context, 'Wq': Wq, 'Wkv': Wkv, 'Wout': Wout, 'mask': mask}
    _L1_xattn_all = _L1_xattn_setup()
    _L1_xattn_in = {k: v for k, v in _L1_xattn_all.items() if k in ('Wq', 'Wkv', 'Wout')}
    del _L1_xattn_all

    def _L1_ffn_setup():
        import jax, jax.numpy as jnp
        import numpy as np
        B, S, D_MODEL, D_HIDDEN = (4, 512, 256, 1024)

        def act_quant(x):
            scale = 127.0 / jnp.clip(jnp.max(jnp.abs(x), axis=-1, keepdims=True), 1e-05)
            return jnp.clip(jnp.round(x * scale), -128, 127) / scale

        def weight_quant(w):
            scale = 1.0 / jnp.clip(jnp.mean(jnp.abs(w)), 1e-05)
            return jnp.clip(jnp.round(w * scale), -1, 1) / scale

        def bit_linear(x, w):
            xq = x + jax.lax.stop_gradient(act_quant(x) - x)
            wq = w + jax.lax.stop_gradient(weight_quant(w) - w)
            return jnp.einsum('bsd,hd->bsh', xq, wq)

        def depthwise_conv1d(x_bcl, w, b):
            y = jax.lax.conv_general_dilated(x_bcl, w, window_strides=(1,), padding=[(1, 1)], dimension_numbers=('NCH', 'OIH', 'NCH'), feature_group_count=x_bcl.shape[1])
            return y + b[None, :, None]
        key = jax.random.key(seed)
        ks = jax.random.split(key, 5)
        lim1 = 1.0 / np.sqrt(D_MODEL)
        lim2 = 1.0 / np.sqrt(D_HIDDEN)
        limc = 1.0 / np.sqrt(3.0)
        return {'x': jax.random.normal(ks[0], (B, S, D_MODEL), dtype=jnp.float32), 'w1': jax.random.uniform(ks[1], (D_HIDDEN, D_MODEL), jnp.float32, -lim1, lim1), 'conv_w': jax.random.uniform(ks[2], (D_HIDDEN, 1, 3), jnp.float32, -limc, limc), 'conv_b': jax.random.uniform(ks[3], (D_HIDDEN,), jnp.float32, -limc, limc), 'w2': jax.random.uniform(ks[4], (D_MODEL, D_HIDDEN), jnp.float32, -lim2, lim2)}
    _L1_ffn_all = _L1_ffn_setup()
    _L1_ffn_in = {k: v for k, v in _L1_ffn_all.items() if k in ('w1', 'conv_w', 'conv_b', 'w2')}
    del _L1_ffn_all
    return {'x': x, 'ctx_1024': ctx_1024, 'mask_SxS2_fk0': mask_SxS2_fk0, 'L0_xattn_w_q': _L0_xattn_in['w_q'], 'L0_xattn_b_q': _L0_xattn_in['b_q'], 'L0_xattn_w_kv': _L0_xattn_in['w_kv'], 'L0_xattn_b_kv': _L0_xattn_in['b_kv'], 'L0_xattn_w_out': _L0_xattn_in['w_out'], 'L0_xattn_b_out': _L0_xattn_in['b_out'], 'L0_ffn_centroids': _L0_ffn_in['centroids'], 'L0_ffn_Wp': _L0_ffn_in['Wp'], 'L0_ffn_bp': _L0_ffn_in['bp'], 'L0_ffn_W1': _L0_ffn_in['W1'], 'L0_ffn_b1': _L0_ffn_in['b1'], 'L0_ffn_W2': _L0_ffn_in['W2'], 'L0_ffn_b2': _L0_ffn_in['b2'], 'L1_xattn_Wq': _L1_xattn_in['Wq'], 'L1_xattn_Wkv': _L1_xattn_in['Wkv'], 'L1_xattn_Wout': _L1_xattn_in['Wout'], 'L1_ffn_w1': _L1_ffn_in['w1'], 'L1_ffn_conv_w': _L1_ffn_in['conv_w'], 'L1_ffn_conv_b': _L1_ffn_in['conv_b'], 'L1_ffn_w2': _L1_ffn_in['w2']}

def reference(x, ctx_1024, mask_SxS2_fk0, L0_xattn_w_q, L0_xattn_b_q, L0_xattn_w_kv, L0_xattn_b_kv, L0_xattn_w_out, L0_xattn_b_out, L0_ffn_centroids, L0_ffn_Wp, L0_ffn_bp, L0_ffn_W1, L0_ffn_b1, L0_ffn_W2, L0_ffn_b2, L1_xattn_Wq, L1_xattn_Wkv, L1_xattn_Wout, L1_ffn_w1, L1_ffn_conv_w, L1_ffn_conv_b, L1_ffn_w2):
    import jax
    import jax.numpy as jnp

    def _L0_xattn_ref(q, kv, w_q, b_q, w_kv, b_kv, w_out, b_out):
        import jax, jax.numpy as jnp
        import numpy as np
        EMBED_DIM = 256
        NUM_HEADS = 16
        HEAD_DIM = EMBED_DIM // NUM_HEADS
        SCALE = HEAD_DIM ** (-0.5)
        B, Nq, C = q.shape
        _, Nkv, _ = kv.shape
        H, D = (NUM_HEADS, HEAD_DIM)
        qp = (q @ w_q + b_q).reshape(B, Nq, H, D).transpose(0, 2, 1, 3)
        kvp = (kv @ w_kv + b_kv).reshape(B, Nkv, 2, H, D).transpose(2, 0, 3, 1, 4)
        kp, vp = (kvp[0], kvp[1])
        attn = jnp.einsum('bhqd,bhkd->bhqk', qp, kp) * SCALE
        attn = jax.nn.softmax(attn, axis=-1)
        out = jnp.einsum('bhqk,bhkd->bhqd', attn, vp)
        out = out.transpose(0, 2, 1, 3).reshape(B, Nq, C)
        return out @ w_out + b_out

    def _L0_ffn_ref(x, centroids, Wp, bp, W1, b1, W2, b2):
        import jax, jax.numpy as jnp
        import numpy as np
        import math
        MAX_NORM = 0.95
        CURVATURE = 1.0
        TOP_K = 2
        EPS = 1e-07

        def _project_to_ball(x):
            norm = jnp.clip(jnp.linalg.norm(x, axis=-1, keepdims=True), EPS, None)
            scale = jnp.where(norm > MAX_NORM, MAX_NORM / norm, jnp.ones_like(norm))
            return x * scale
        B, N, D = x.shape
        E = centroids.shape[0]
        x_hyper = _project_to_ball(x @ Wp + bp)
        c_proj = _project_to_ball(centroids)
        x_norm_sq = jnp.sum(x_hyper * x_hyper, axis=-1)
        c_norm_sq = jnp.sum(c_proj * c_proj, axis=-1)
        x_norm_sq = jnp.clip(x_norm_sq, None, 0.99)
        c_norm_sq = jnp.clip(c_norm_sq, None, 0.99)
        dot = jnp.einsum('bnd,ed->bne', x_hyper, c_proj)
        diff_sq = jnp.maximum(x_norm_sq[..., None] + c_norm_sq - 2.0 * dot, 0.0)
        denom = (1.0 - x_norm_sq)[..., None] * (1.0 - c_norm_sq) + EPS
        arg = jnp.clip(1.0 + 2.0 * diff_sq / denom, 1.0 + EPS, None)
        dist = jnp.arccosh(arg)
        routing_logits = -dist / math.sqrt(CURVATURE)
        top_v, top_i = jax.lax.top_k(routing_logits, TOP_K)
        top_w = jax.nn.softmax(top_v, axis=-1)
        comb = jnp.sum(jax.nn.one_hot(top_i, E, dtype=x.dtype) * top_w[..., None], axis=2)
        h = jax.nn.gelu(jnp.einsum('bnd,edf->bnef', x, W1) + b1, approximate=False)
        y = jnp.einsum('bnef,efd->bned', h, W2) + b2
        out = jnp.einsum('bne,bned->bnd', comb, y)
        return out

    def _L1_xattn_ref(query, context, Wq, Wkv, Wout, mask):
        import jax, jax.numpy as jnp
        import numpy as np
        B, S, D, H = (2, 512, 256, 16)
        A = D // H
        NEG = -1000000000.0
        b, q_len, d = query.shape
        c_len = context.shape[1]
        h, a = (H, A)
        scale = 1.0 / np.sqrt(d)
        q = query @ Wq.T
        kv = context @ Wkv.T
        k, v = jnp.split(kv, 2, axis=-1)
        q = q.reshape(b, q_len, h, a)
        k = k.reshape(b, c_len, h, a)
        v = v.reshape(b, c_len, h, a)
        scores = jnp.einsum('bqha,bkha->bqkh', q, k)
        scores = scores + mask[None, :, :, None]
        attn = jax.nn.softmax(scores * scale, axis=2)
        out = jnp.einsum('bqkh,bkha->bqha', attn, v).reshape(b, q_len, d)
        return out @ Wout.T

    def _L1_ffn_ref(x, w1, conv_w, conv_b, w2):
        import jax, jax.numpy as jnp
        import numpy as np
        B, S, D_MODEL, D_HIDDEN = (4, 512, 256, 1024)

        def act_quant(x):
            scale = 127.0 / jnp.clip(jnp.max(jnp.abs(x), axis=-1, keepdims=True), 1e-05)
            return jnp.clip(jnp.round(x * scale), -128, 127) / scale

        def weight_quant(w):
            scale = 1.0 / jnp.clip(jnp.mean(jnp.abs(w)), 1e-05)
            return jnp.clip(jnp.round(w * scale), -1, 1) / scale

        def bit_linear(x, w):
            xq = x + jax.lax.stop_gradient(act_quant(x) - x)
            wq = w + jax.lax.stop_gradient(weight_quant(w) - w)
            return jnp.einsum('bsd,hd->bsh', xq, wq)

        def depthwise_conv1d(x_bcl, w, b):
            y = jax.lax.conv_general_dilated(x_bcl, w, window_strides=(1,), padding=[(1, 1)], dimension_numbers=('NCH', 'OIH', 'NCH'), feature_group_count=x_bcl.shape[1])
            return y + b[None, :, None]
        h = bit_linear(x, w1)
        h = depthwise_conv1d(h.transpose(0, 2, 1), conv_w, conv_b)
        h = h.transpose(0, 2, 1)
        h = jax.nn.silu(h)
        return bit_linear(h, w2)
    x = x + _L0_xattn_ref(_layernorm(x, axis=-1), ctx_1024, L0_xattn_w_q, L0_xattn_b_q, L0_xattn_w_kv, L0_xattn_b_kv, L0_xattn_w_out, L0_xattn_b_out)
    x = x + _L0_ffn_ref(_layernorm(x, axis=-1), L0_ffn_centroids, L0_ffn_Wp, L0_ffn_bp, L0_ffn_W1, L0_ffn_b1, L0_ffn_W2, L0_ffn_b2)
    x = x + _L1_xattn_ref(_layernorm(x, axis=-1), ctx_1024, L1_xattn_Wq, L1_xattn_Wkv, L1_xattn_Wout, mask_SxS2_fk0)
    x = x + _L1_ffn_ref(_layernorm(x, axis=-1), L1_ffn_w1, L1_ffn_conv_w, L1_ffn_conv_b, L1_ffn_w2)
    return x

_drawn_inputs = setup_inputs


def setup_inputs(seed=0):
    import zlib

    import numpy as np

    out = dict(_drawn_inputs(seed))
    spreads = {'L0_xattn_b_q': (0.0, 0.387),
     'L0_xattn_b_kv': (0.0, 0.1),
     'L0_xattn_b_out': (0.0, 0.1),
     'L0_ffn_bp': (0.0, 0.1),
     'L0_ffn_b1': (0.0, 0.404),
     'L0_ffn_b2': (0.0, 0.1)}
    factors = {}
    for name, (base, spread) in spreads.items():
        noise = np.random.default_rng([zlib.crc32(name.encode()), seed]).standard_normal(out[name].shape)
        drawn = base * np.exp(spread * noise) if base else spread * noise
        out[name] = jnp.asarray(drawn.astype(out[name].dtype))
    for name, factor in factors.items():
        out[name] = (out[name] * factor).astype(out[name].dtype)
    return out
```

```python
import concourse.bass as bass
from concourse import mybir
from contextlib import ExitStack

F32 = mybir.dt.float32
F32R = mybir.dt.float32r
BF16 = mybir.dt.bfloat16
ALU = mybir.AluOpType
ACT = mybir.ActivationFunctionType
AX = mybir.AxisListType

B, S, D = 8, 112, 256
H, DH = 16, 16
SK = 375
SKP = SK + 1
KC, KP = 3, 125
T = B * S
DC = D // 128
HALF = T // 2
HP = H // 2
NS = 3 * DH
NSM = NS + 2
E, F = 8, 1024
FC = F // 128
LN_EPS = 1e-5
AV0, E0, O0, X0, Y0, R0 = 2, 2, 1, 1, 1, 2
GROUPS = 4


def head_of(group, n):
    return 4 * (group // 2) + n, group % 2


class Batch:

    def __init__(self, pair, parity):
        self.pair, self.parity = pair, parity

    def plus(self, n):
        at = self.parity + n
        return Batch(self.pair + at // 2, at % 2) if at // 2 else Batch(self.pair, at % 2)

    def count(self, per_batch, within):
        return self.pair * (2 * per_batch) + (self.parity * per_batch + within)

    def own(self, per_batch):
        return self.pair * per_batch + per_batch

    def index(self):
        return self.pair * 2 + self.parity


def product3(nc, out, w, x, first=True, last=True):
    ins = None
    for k, ((wh, wl), (xh, xl)) in enumerate(zip(w, x)):
        for n, (a, b) in enumerate(((wh, xh), (wh, xl), (wl, xh))):
            ins = nc.tensor.matmul(out, a, b, start=first and k == 0 and n == 0,
                                   stop=last and k == len(w) - 1 and n == 2)
    return ins


def xattn_ffn_kernel(nc, x, ctx, mask, w_q0, b_q0, w_kv0, b_kv0, w_out0, b_out0, centroids, w_p, b_p,
                     w_1, b_1, w_2, b_2, w_q1, w_kv1, w_out1, w_up, conv_w, conv_b, w_down, out):
    main = ExitStack()
    scope = [main]

    def sb(name, shape, dt=F32):
        return scope[-1].enter_context(nc.sbuf_tensor(name, shape, dt))

    def pb(name, shape=(128, 512), dt=F32):
        return scope[-1].enter_context(nc.psum_tensor(name, list(shape), dt))

    phase_sems = []

    def sem(name):
        phase_sems.append(nc.alloc_semaphore(name))
        return phase_sems[-1]

    def end_phase():
        nc.clear_and_free_semaphores(list(phase_sems))
        phase_sems.clear()
        nc.all_engine_barrier()
        scope.pop()

    q_dram = nc.dram_tensor("q_parts", (2, D, B, S), F32)
    k_dram = [nc.dram_tensor(f"k_parts{j}", (2, D, SKP), F32) for j in range(2)]

    with main:
        x_sb = sb("x_sb", [S, B, D])
        ident = sb("ident", [128, 128])
        ident_r = sb("ident_r", [128, 4 * S], F32R)
        ones = sb("ones", [128, 128])
        xn = sb("xn", [S, B, D])
        xnt = sb("xnt", [128, 2, DC, T], F32R)

        setup = ExitStack()
        scope.append(setup)
        with setup:
            x_in = sem("x_in")
            id_zero = sem("id_zero")
            id_done = sem("id_done")
            idr_done = sem("idr_done")
            with nc.Block() as block:
                @block.sync
                def _(sp):
                    sp.dma_start(x_sb[:], x.rearrange("b s d -> s b d")).then_inc(x_in, 16)
                    sp.wait_ge(x_in, 16)

                @block.gpsimd
                def _(pool):
                    nc.gpsimd.memset(ident[:], 0.0).then_inc(id_zero, 1)
                    nc.gpsimd.memset(ones[:], 1.0).then_inc(id_zero, 1)
                    pool.wait_ge(id_zero, 1)
                    nc.gpsimd.affine_select(out=ident[:], in_=ident[:], compare_op=ALU.not_equal, fill=1.0,
                                            base=0, pattern=[[-1, 128]], channel_multiplier=1).then_inc(id_done, 1)

                @block.vector
                def _(dve):
                    dve.wait_ge(id_done, 1)
                    for n in range(4):
                        nc.vector.tensor_copy(ident_r[:, n * S:(n + 1) * S], ident[:, 0:S]).then_inc(idr_done, 1)
        end_phase()

        def layer_norm(tag, squares):
            sums = sb(f"{tag}_sums", [S, B])
            var = sb(f"{tag}_var", [S, B])
            root = sb(f"{tag}_root", [S, B])
            rstd = sb(f"{tag}_rstd", [S, B])
            centred = sem(f"{tag}_centred")
            squared = sem(f"{tag}_squared")
            var_ready = sem(f"{tag}_var_ready")
            root_ready = sem(f"{tag}_root_ready")
            xn_ready = sem(f"{tag}_xn_ready")

            def wide(a):
                return a[:].rearrange("p (b o) -> p b o", o=1).broadcast_to([S, B, D])

            def dve_steps(dve, link):
                link(nc.vector.tensor_reduce(sums[:], x_sb[:], AX.X, ALU.add))
                link(nc.vector.tensor_scalar(sums[:], sums[:], 1.0 / D, None, ALU.mult))
                nc.vector.tensor_tensor(xn[:], x_sb[:], wide(sums), ALU.subtract).then_inc(centred, 1)
                dve.wait_ge(squared, 1)
                link(nc.vector.tensor_reduce(var[:], squares, AX.X, ALU.add))
                nc.vector.tensor_scalar(var[:], var[:], 1.0 / D, LN_EPS, ALU.mult, ALU.add).then_inc(var_ready, 1)
                dve.wait_ge(root_ready, 1)
                link(nc.vector.reciprocal(rstd[:], root[:]))
                dve.wait_ge(centred, 1)
                nc.vector.tensor_tensor(xn[:], xn[:], wide(rstd), ALU.mult).then_inc(xn_ready, 1)

            def act_steps(act):
                act.wait_ge(centred, 1)
                nc.scalar.activation(squares, xn[:], ACT.Square).then_inc(squared, 1)
                act.wait_ge(var_ready, 1)
                nc.scalar.activation(root[:], var[:], ACT.Sqrt).then_inc(root_ready, 1)

            return dve_steps, act_steps, xn_ready

        def chain(name):
            s = sem(name)
            n = [0]

            def bind(eng):
                def link(ins):
                    n[0] += 1
                    ins.then_inc(s, 1)
                    eng.wait_ge(s, n[0])
                return link
            return bind

        def queries(tag, loads, transposed, bias_q):
            st = ExitStack()
            scope.append(st)
            with st:
                w_in = sem(f"{tag}_w_in")
                wt_ps = sem(f"{tag}_wt_ps")
                wt_out = sem(f"{tag}_wt_out")
                w_hi = sem(f"{tag}_w_hi")
                w_lo = sem(f"{tag}_w_lo")
                t_ps = sem(f"{tag}_t_ps")
                t_hi = sem(f"{tag}_t_hi")
                t_lo = sem(f"{tag}_t_lo")
                q_ps = sem(f"{tag}_q_ps")
                q_f = sem(f"{tag}_q_f")
                q_hi = sem(f"{tag}_q_hi")
                q_lo = sem(f"{tag}_q_lo")
                q_out = sem(f"{tag}_q_out")
                bias_in = sem(f"{tag}_bias_in")
                n_loads = len(loads)
                nat = sb(f"{tag}_nat", [128, 4, DC, D]) if transposed else None
                bq = sb(f"{tag}_bq", [128, DC])
                qf = sb(f"{tag}_qf", [128, DC, T])
                qp = sb(f"{tag}_qp", [128, 2, DC, T], F32R)
                banks = [pb(f"{tag}_bank{i}") for i in range(4)]
                link_dve = chain(f"{tag}_dve_chain")
                ln_dve, ln_act, xn_ready = layer_norm(tag, sb(f"{tag}_squares", [S, B, D])[:])
                target = nat if transposed else w_attn

                with nc.Block() as block:
                    @block.sync
                    def _(sp):
                        for which, src in loads:
                            sp.dma_start(target[:, which], src).then_inc(w_in, 16)
                        if bias_q is not None:
                            sp.dma_start(bq[:], bias_q.rearrange("(c p) -> p c", p=128), allow_slow_non_contiguous=True).then_inc(bias_in, 16)
                        for n, ready in enumerate((q_hi, q_lo)):
                            sp.wait_ge(ready, 2 * DC)
                            sp.dma_start(q_dram[n].rearrange("(c p) b s -> p c (b s)", p=128),
                                         qp[:, n].bitcast(F32)).then_inc(q_out, 16)
                        sp.wait_ge(q_out, 32)

                    @block.scalar
                    def _(act):
                        ln_act(act)
                        if transposed:
                            for n in range(8):
                                act.wait_ge(wt_ps, n + 1)
                                nc.scalar.activation(w_attn[:, n // 2, n % 2, :], banks[n % 4][:, 0:D],
                                                     ACT.Copy).then_inc(wt_out, 1)
                        for n in range(4):
                            c, half = n // 2, n % 2
                            act.wait_ge(t_ps, n + 1)
                            nc.scalar.activation(xnt[:, 0, c, half * HALF:(half + 1) * HALF],
                                                 banks[n][:, 0:HALF], ACT.Copy).then_inc(t_hi, 1)
                        if bias_q is not None:
                            act.wait_ge(bias_in, 16)
                        for n in range(4):
                            m, half = n // 2, n % 2
                            act.wait_ge(q_ps, n + 1)
                            dst = qf[:, m, half * HALF:(half + 1) * HALF]
                            if bias_q is not None:
                                nc.scalar.activation(dst, banks[n][:, 0:HALF], ACT.Identity,
                                                     bias=bq[:, m:m + 1]).then_inc(q_f, 1)
                            else:
                                nc.scalar.activation(dst, banks[n][:, 0:HALF], ACT.Copy).then_inc(q_f, 1)

                    @block.gpsimd
                    def _(pool):
                        if transposed:
                            pool.wait_ge(wt_out, 8)
                        else:
                            pool.wait_ge(w_in, 16 * n_loads)
                        nc.gpsimd.tensor_copy(wr_attn[:, 0], w_attn[:]).then_inc(w_hi, 1)
                        pool.wait_ge(w_hi, 1)
                        nc.gpsimd.tensor_tensor(wr_attn[:, 1], w_attn[:], wr_attn[:, 0].bitcast(F32),
                                                ALU.subtract).then_inc(w_lo, 1)

                    @block.vector
                    def _(dve):
                        ln_dve(dve, link_dve(dve))
                        for n in range(4):
                            c, half = n // 2, n % 2
                            cols = slice(half * HALF, (half + 1) * HALF)
                            dve.wait_ge(t_hi, n + 1)
                            nc.vector.tensor_tensor(xnt[:, 1, c, cols], banks[n][:, 0:HALF],
                                                    xnt[:, 0, c, cols].bitcast(F32),
                                                    ALU.subtract).then_inc(t_lo, 1)
                        for n in range(4):
                            m, half = n // 2, n % 2
                            cols = slice(half * HALF, (half + 1) * HALF)
                            dve.wait_ge(q_f, n + 1)
                            nc.vector.tensor_copy(qp[:, 0, m, cols], qf[:, m, cols]).then_inc(q_hi, 1)
                            dve.wait_ge(q_hi, n + 1)
                            nc.vector.tensor_tensor(qp[:, 1, m, cols], qf[:, m, cols],
                                                    qp[:, 0, m, cols].bitcast(F32),
                                                    ALU.subtract).then_inc(q_lo, 1)

                    @block.tensor
                    def _(pe):
                        if transposed:
                            pe.wait_ge(w_in, 16 * n_loads)
                            for n in range(8):
                                which, c = n // 2, n % 2
                                if n >= 4:
                                    pe.wait_ge(wt_out, n - 3)
                                for o in range(DC):
                                    last = nc.tensor.transpose(banks[n % 4][:, o * 128:(o + 1) * 128],
                                                               nat[:, which, o, c * 128:(c + 1) * 128], ident[:])
                                last.then_inc(wt_ps, 1)
                            pe.wait_ge(wt_out, 8)
                        pe.wait_ge(xn_ready, 1)
                        for n in range(4):
                            c, half = n // 2, n % 2
                            for b in range(4):
                                last = nc.tensor.transpose(banks[n][:, b * S:(b + 1) * S],
                                                           xn[:, 4 * half + b, c * 128:(c + 1) * 128],
                                                           ident[0:S, 0:S])
                            last.then_inc(t_ps, 1)
                        pe.wait_ge(w_lo, 1)
                        pe.wait_ge(t_lo, 4)
                        for n in range(4):
                            m, half = n // 2, n % 2
                            cols = slice(half * HALF, (half + 1) * HALF)
                            ms = slice(m * 128, (m + 1) * 128)
                            product3(nc, banks[n][:, 0:HALF],
                                     [(wr_attn[:, 0, 0, k, ms], wr_attn[:, 1, 0, k, ms]) for k in range(DC)],
                                     [(xnt[:, 0, k, cols], xnt[:, 1, k, cols]) for k in range(DC)]).then_inc(q_ps, 1)
            end_phase()

        def attention(tag, scale, bias_kv, bias_out, mask):
            st = ExitStack()
            scope.append(st)
            with st:
                ctx_sb = sb(f"{tag}_ctx", [KP, 2, KC, D])
                ct = sb(f"{tag}_ct", [128, 2, DC, SKP], F32R)
                kf = sb(f"{tag}_kf", [128, DC, SKP])
                kp = sb(f"{tag}_kp", [128, 2, DC, SKP], F32R)
                kst = sb(f"{tag}_kst", [128, 2, HP, SKP], F32R)
                qst = sb(f"{tag}_qst", [128, 2, HP, S], F32R)
                q2 = sb(f"{tag}_q2", [128, HP, S], F32R)
                vx = sb(f"{tag}_v", [KP, 2, KC, H, 32])
                mx = sb(f"{tag}_mx", [S, HP, 2])
                mparts = sb(f"{tag}_mparts", [S, HP, 2, 64], F32R)
                es = sb(f"{tag}_e", [KP, 2, KC, 4 * S])
                rsum = sb(f"{tag}_rsum", [S, H])
                avs = sb(f"{tag}_avs", [128, GROUPS * S])
                o_sb = sb(f"{tag}_o", [S, H, DH])
                ot = sb(f"{tag}_ot", [128, 2, DC, S], F32R)
                bk = sb(f"{tag}_bk", [128, DC])
                bv = sb(f"{tag}_bv", [KP, D])
                bo = sb(f"{tag}_bo", [1, D])
                mask_sb = sb(f"{tag}_mask", [S, SK])
                mask_r = sb(f"{tag}_mask_r", [S, 2, SK], F32R)
                masked = sb(f"{tag}_masked", [S, 2, SK])
                prep = [pb(f"{tag}_prep{i}") for i in range(2)]
                s1 = [pb(f"{tag}_s1_{i}") for i in range(2)]
                s2 = [pb(f"{tag}_s2_{i}") for i in range(2)]
                av = pb(f"{tag}_av")
                small = pb(f"{tag}_small")

                const_in = sem(f"{tag}_const_in")
                filled = sem(f"{tag}_filled")
                mask_parts = sem(f"{tag}_mask_parts")
                ctx_in = [sem(f"{tag}_ctx_in{j}") for j in range(2)]
                kst_in = [sem(f"{tag}_kst_in{j}") for j in range(2)]
                qst_in = [sem(f"{tag}_qst_in{j}") for j in range(2)]
                k_stored = sem(f"{tag}_k_stored")
                ct_ps = sem(f"{tag}_ct_ps")
                ct_hi = sem(f"{tag}_ct_hi")
                ct_lo = sem(f"{tag}_ct_lo")
                k_ps = sem(f"{tag}_k_ps")
                k_f = sem(f"{tag}_k_f")
                k_hi = sem(f"{tag}_k_hi")
                k_lo = sem(f"{tag}_k_lo")
                v_ps = sem(f"{tag}_v_ps")
                v_out = sem(f"{tag}_v_out")
                s1_ps = sem(f"{tag}_s1_ps")
                max_out = sem(f"{tag}_max_out")
                max_hi = sem(f"{tag}_max_hi")
                max_lo = sem(f"{tag}_max_lo")
                m_ps = sem(f"{tag}_m_ps")
                s2_ps = sem(f"{tag}_s2_ps")
                e_out = sem(f"{tag}_e_out")
                av_ps = sem(f"{tag}_av_ps")
                avs_out = sem(f"{tag}_avs_out")
                avt_ps = sem(f"{tag}_avt_ps")
                rsum_out = sem(f"{tag}_rsum_out")
                o_out = sem(f"{tag}_o_out")
                ot_ps = sem(f"{tag}_ot_ps")
                ot_hi = sem(f"{tag}_ot_hi")
                y_ps = sem(f"{tag}_y_ps")
                q2_out = sem(f"{tag}_q2_out")
                ot_lo = sem(f"{tag}_ot_lo")
                x_added = sem(f"{tag}_x_added")
                tick = sb(f"{tag}_tick", [1, 8])
                n_const = 48 if bias_kv is not None else 16
                n_fill = 4 + 4 + 3

                def half_view(tile, j, hi):
                    return tile[64 * hi:64 * hi + 64, j]

                with nc.Block() as block:
                    @block.sync
                    def _(sp):
                        if mask is not None:
                            sp.dma_start(mask_sb[:], mask).then_inc(const_in, 16)
                        else:
                            sp.dma_start(bk[:], bias_kv[0:D].rearrange("(c p) -> p c", p=128), allow_slow_non_contiguous=True).then_inc(const_in, 16)
                            sp.dma_start(bv[:], bias_kv[D:2 * D].rearrange("(o n) -> o n", o=1)
                                         .broadcast_to([KP, D])).then_inc(const_in, 16)
                            sp.dma_start(bo[:], bias_out.rearrange("(o n) -> o n", o=1)).then_inc(const_in, 16)

                        def load_ctx(b, at):
                            src = ctx[bass.ds(at, 1)].rearrange("o (c p) d -> p (o c) d", p=KP)
                            sp.dma_start(ctx_sb[:, b.parity], src).then_inc(ctx_in[b.parity], 16)

                        def load_q(b, at):
                            for hi in range(2):
                                for slot, part in enumerate((0, 0, 1)):
                                    src = q_dram[part][:, bass.ds(at, 1), :]
                                    src = src.rearrange("(t e d) o q -> e d (t o) q", e=2, d=DH)[hi]
                                    row = 64 * hi + DH * slot
                                    sp.dma_start(qst[row:row + DH, b.parity].bitcast(F32), src)\
                                        .then_inc(qst_in[b.parity], 16)

                        def store_k(b, parts_done):
                            for part, ready in enumerate((k_hi, k_lo)):
                                sp.wait_ge(ready, parts_done)
                                sp.dma_start(k_dram[b.parity][part].rearrange("(c p) n -> p c n", p=128),
                                             kp[:, part].bitcast(F32)).then_inc(k_stored, 16)

                        def load_k(b, stored):
                            sp.wait_ge(k_stored, stored)
                            for hi in range(2):
                                for slot, part in enumerate((0, 1, 0)):
                                    src = k_dram[b.parity][part].rearrange("(t e d) n -> e d t n", e=2, d=DH)[hi]
                                    row = 64 * hi + DH * slot
                                    sp.dma_start(kst[row:row + DH, b.parity].bitcast(F32), src)\
                                        .then_inc(kst_in[b.parity], 16)

                        sp.wait_ge(filled, n_fill)
                        for b in (Batch(0, 0), Batch(0, 1)):
                            load_ctx(b, b.index())
                            load_q(b, b.index())
                        for b in (Batch(0, 0), Batch(0, 1)):
                            store_k(b, b.count(DC, DC))
                            load_k(b, b.count(32, 32))

                        names = iter(range(100))

                        def held(value):
                            register = sp.alloc_register(f"{tag}_held{next(names)}")
                            sp.reg_mov(register, value)
                            return register

                        with sp.Fori(0, B // 2 - 1) as pair:
                            for parity in range(2):
                                b = Batch(pair, parity)
                                ahead = b.plus(2)
                                batch = sp.snap(held(ahead.index()), min_val=0, max_val=B - 1)
                                transposed_b = held(b.count(DC, DC))
                                q2_b = held(b.count(2, 2))
                                s1_b = held(b.count(H, H))
                                kst_b = held(b.own(96))
                                parts_ahead = held(ahead.count(DC, DC))
                                s2_b = held(b.count(GROUPS * KC, GROUPS * KC))
                                stored_ahead = held(ahead.count(32, 32))
                                sp.wait_ge(ct_ps, transposed_b)
                                load_ctx(ahead, batch)
                                sp.wait_ge(q2_out, q2_b)
                                sp.wait_ge(s1_ps, s1_b)
                                load_q(ahead, batch)
                                sp.wait_ge(kst_in[parity], kst_b)
                                store_k(ahead, parts_ahead)
                                sp.wait_ge(s2_ps, s2_b)
                                load_k(ahead, stored_ahead)

                    @block.scalar
                    def _(act):
                        def exps(b, g):
                            for kc in range(KC):
                                act.wait_ge(s2_ps, b.count(GROUPS * KC, g * KC + kc + 1))
                                if kc == 0:
                                    act.wait_ge(av_ps, b.count(GROUPS, AV0 + g - 1))
                                nc.scalar.activation(es[:, g % 2, kc, :], s2[(g * KC + kc) % 2][0:KP, 0:4 * S],
                                                     ACT.Exp, scale=scale).then_inc(e_out, 1)

                        def output(b):
                            act.wait_ge(av_ps, b.count(GROUPS, AV0 + GROUPS))
                            nc.scalar.activation(avs[:], av[:, 0:GROUPS * S], ACT.Copy).then_inc(avs_out, 1)
                            act.wait_ge(ot_ps, b.count(1, 1))
                            nc.scalar.activation(ot[:, 0].rearrange("p c q -> p (c q)"), small[:, 0:DC * S],
                                                 ACT.Copy).then_inc(ot_hi, 1)

                        def prepare(b, first):
                            for c in range(DC):
                                act.wait_ge(ct_ps, b.count(DC, c + 1))
                                nc.scalar.activation(ct[:, 0, c, 0:SK], prep[c][:, 0:SK], ACT.Copy).then_inc(ct_hi, 1)
                            for m in range(DC):
                                act.wait_ge(k_ps, b.count(DC, m + 1))
                                if not first:
                                    act.wait_ge(k_lo, b.count(DC, 0))
                                if bias_kv is not None:
                                    nc.scalar.activation(kf[:, m], prep[m][:, 0:SKP], ACT.Identity,
                                                         bias=bk[:, m:m + 1]).then_inc(k_f, 1)
                                else:
                                    nc.scalar.activation(kf[:, m], prep[m][:, 0:SKP], ACT.Copy).then_inc(k_f, 1)

                        act.wait_ge(filled, n_fill)
                        act.wait_ge(const_in, n_const)
                        for n in range(E0):
                            nc.scalar.activation(tick[:, 4 + n:5 + n], ones[0:1, 0:1], ACT.Exp).then_inc(e_out, 1)
                        prepare(Batch(0, 0), True)
                        prepare(Batch(0, 1), False)

                        def turn(b, ahead):
                            for g in range(GROUPS):
                                exps(b, g)
                            output(b)
                            if ahead:
                                prepare(b.plus(2), False)

                        with act.Fori(0, B // 2 - 1) as pair:
                            for parity in range(2):
                                turn(Batch(pair, parity), True)
                        turn(Batch(B // 2 - 1, 0), False)
                        turn(Batch(B // 2 - 1, 1), False)

                    @block.vector
                    def _(dve):
                        def maxima(b, g):
                            for n in range(4):
                                t, hi = head_of(g, n)
                                i = 4 * g + n
                                dve.wait_ge(s1_ps, b.count(H, i + 1))
                                if mask is not None:
                                    nc.vector.memset(tick[:, i % 2:i % 2 + 1], 0.0)
                                    nc.vector.tensor_tensor_reduce(
                                        out=masked[:, i % 2], in0=s1[i % 2][0:S, 0:SK], in1=mask_sb[:], scale=1.0,
                                        scalar=-3.0e38, op0=ALU.add, op1=ALU.max,
                                        accum_out=mx[:, t, hi:hi + 1]).then_inc(max_out, 1)
                                else:
                                    nc.vector.reduce_max(mx[:, t, hi:hi + 1], s1[i % 2][0:S, 0:SK], AX.X)\
                                        .then_inc(max_out, 1)

                        def shift(b):
                            dve.wait_ge(max_out, b.count(H, H))
                            nc.vector.tensor_copy(mparts[:, :, :, NS], mx[:]).then_inc(max_hi, 1)
                            dve.wait_ge(max_hi, b.count(1, 1))
                            nc.vector.tensor_tensor(mparts[:, :, :, NS + 1], mx[:], mparts[:, :, :, NS].bitcast(F32),
                                                    ALU.subtract).then_inc(max_lo, 1)
                            dve.wait_ge(qst_in[b.parity], b.own(96))
                            for n in range(2):
                                dve.wait_ge(m_ps, b.count(2, n + 1))
                                nc.vector.tensor_tensor(
                                    q2[:, 4 * n:4 * n + 4, :], qst[:, b.parity, 4 * n:4 * n + 4, :].bitcast(F32),
                                    small[:, 0:4 * S].rearrange("p (t q) -> p t q", t=4),
                                    ALU.subtract).then_inc(q2_out, 1)

                        def output(b):
                            dve.wait_ge(avt_ps, b.count(1, 1))
                            heads = small[0:S, :].rearrange("p (h r) -> p h r", r=32)
                            nc.vector.reciprocal(rsum[:], heads[:, :, DH]).then_inc(rsum_out, 1)
                            dve.wait_ge(rsum_out, b.count(1, 1))
                            by_half = o_sb[:].rearrange("p (a n e) d -> p a e n d", n=4, e=2)
                            for g in range(GROUPS):
                                ins = nc.vector.tensor_tensor(
                                    by_half[:, g // 2, g % 2], heads[:, 4 * g:4 * g + 4, 0:DH],
                                    rsum[:, 4 * g:4 * g + 4].rearrange("p (h o) -> p h o", o=1)
                                    .broadcast_to([S, 4, DH]), ALU.mult)
                            ins.then_inc(o_out, 1)
                            dve.wait_ge(ot_hi, b.count(1, 1))
                            nc.vector.tensor_tensor(ot[:, 1].rearrange("p c q -> p (c q)"), small[:, 0:DC * S],
                                                    ot[:, 0].rearrange("p c q -> p (c q)").bitcast(F32),
                                                    ALU.subtract).then_inc(ot_lo, 1)
                            dve.wait_ge(y_ps, b.count(1, 1))
                            row = x_sb[:, bass.ds(b.index(), 1), :].rearrange("p o d -> p (o d)")
                            nc.vector.tensor_tensor(row, row, small[0:S, 0:D], ALU.add).then_inc(x_added, 1)

                        def prepare(b, first):
                            for c in range(DC):
                                dve.wait_ge(ct_hi, b.count(DC, c + 1))
                                nc.vector.tensor_tensor(ct[:, 1, c, 0:SK], prep[c][:, 0:SK],
                                                        ct[:, 0, c, 0:SK].bitcast(F32), ALU.subtract).then_inc(ct_lo, 1)
                            for m in range(DC):
                                dve.wait_ge(k_f, b.count(DC, m + 1))
                                if not first:
                                    dve.wait_ge(k_stored, b.count(32, 0))
                                nc.vector.tensor_copy(kp[:, 0, m], kf[:, m]).then_inc(k_hi, 1)
                                dve.wait_ge(k_hi, b.count(DC, m + 1))
                                nc.vector.tensor_tensor(kp[:, 1, m], kf[:, m], kp[:, 0, m].bitcast(F32),
                                                        ALU.subtract).then_inc(k_lo, 1)
                            for kc in range(KC):
                                dve.wait_ge(v_ps, b.count(KC, kc + 1))
                                dst = vx[:, b.parity, kc, :, 0:DH]
                                src = prep[kc % 2][0:KP, 0:D].rearrange("p (h d) -> p h d", h=H)
                                if bias_kv is not None:
                                    nc.vector.tensor_tensor(dst, src, bv[:].rearrange("p (h d) -> p h d", h=H),
                                                            ALU.add).then_inc(v_out, 1)
                                else:
                                    nc.vector.tensor_copy(dst, src).then_inc(v_out, 1)

                        for j in range(2):
                            for row in (32, 96):
                                nc.vector.memset(kst[row:row + 32, j].bitcast(F32), 1.0).then_inc(filled, 1)
                                nc.vector.memset(qst[row:row + 32, j].bitcast(F32), 0.0).then_inc(filled, 1)
                        nc.vector.memset(vx[:], 1.0).then_inc(filled, 1)
                        nc.vector.memset(mparts[:].bitcast(F32), 0.0).then_inc(filled, 1)
                        nc.vector.memset(ct[:].bitcast(F32), 0.0).then_inc(filled, 1)
                        dve.wait_ge(filled, n_fill)
                        dve.wait_ge(const_in, n_const)
                        nc.vector.memset(tick[:, 2:3], 0.0).then_inc(o_out, 1)
                        nc.vector.memset(tick[:, 3:4], 0.0).then_inc(x_added, 1)
                        if mask is not None:
                            nc.vector.tensor_copy(mask_r[:, 0], mask_sb[:]).then_inc(mask_parts, 1)
                            dve.wait_ge(mask_parts, 1)
                            nc.vector.tensor_tensor(mask_r[:, 1], mask_sb[:], mask_r[:, 0].bitcast(F32),
                                                    ALU.subtract).then_inc(mask_parts, 1)
                        prepare(Batch(0, 0), True)
                        prepare(Batch(0, 1), False)
                        for g in range(GROUPS):
                            maxima(Batch(0, 0), g)
                        shift(Batch(0, 0))

                        def turn(b, ahead):
                            if ahead >= 1:
                                for g in range(GROUPS):
                                    maxima(b.plus(1), g)
                                shift(b.plus(1))
                            output(b)
                            if ahead >= 2:
                                prepare(b.plus(2), False)

                        with dve.Fori(0, B // 2 - 1) as pair:
                            for parity in range(2):
                                turn(Batch(pair, parity), 2)
                        turn(Batch(B // 2 - 1, 0), 1)
                        turn(Batch(B // 2 - 1, 1), 0)

                    @block.tensor
                    def _(pe):
                        def first_batch(b):
                            return isinstance(b.pair, int) and b.pair == 0 and b.parity == 0

                        def prepare(b):
                            pe.wait_ge(ctx_in[b.parity], b.own(16))
                            for c in range(DC):
                                if not first_batch(b):
                                    pe.wait_ge(v_out, b.count(KC, -c))
                                for kc in range(KC):
                                    last = nc.tensor.transpose(prep[c][:, kc * KP:(kc + 1) * KP],
                                                               ctx_sb[:, b.parity, kc, c * 128:(c + 1) * 128],
                                                               ident[0:KP, 0:KP])
                                last.then_inc(ct_ps, 1)
                            pe.wait_ge(ct_lo, b.count(DC, DC))
                            for m in range(DC):
                                ms = slice(m * 128, (m + 1) * 128)
                                product3(nc, prep[m][:, 0:SKP],
                                         [(wr_attn[:, 0, 1, k, ms], wr_attn[:, 1, 1, k, ms]) for k in range(DC)],
                                         [(ct[:, 0, k], ct[:, 1, k]) for k in range(DC)]).then_inc(k_ps, 1)
                            for kc in range(KC):
                                if kc < 2:
                                    pe.wait_ge(k_f, b.count(DC, kc + 1))
                                else:
                                    pe.wait_ge(v_out, b.count(KC, 1))
                                ks = slice(kc * KP, (kc + 1) * KP)
                                product3(nc, prep[kc % 2][0:KP, 0:D],
                                         [(ct[:, 0, k, ks], ct[:, 1, k, ks]) for k in range(DC)],
                                         [(wr_attn[:, 0, 2, k], wr_attn[:, 1, 2, k]) for k in range(DC)])\
                                    .then_inc(v_ps, 1)

                        def scores_for_max(b, g):
                            for n in range(4):
                                t, hi = head_of(g, n)
                                i = 4 * g + n
                                if i == 0:
                                    pe.wait_ge(kst_in[b.parity], b.own(96))
                                    pe.wait_ge(qst_in[b.parity], b.own(96))
                                if i >= 2 or not first_batch(b):
                                    pe.wait_ge(max_out, b.count(H, i - 1))
                                rows = slice(64 * hi, 64 * hi + NS)
                                nc.tensor.matmul(s1[i % 2][0:S, 0:SKP], qst[rows, b.parity, t], kst[rows, b.parity, t],
                                                 start=True, stop=True).then_inc(s1_ps, 1)

                        def max_rows(b):
                            pe.wait_ge(max_lo, b.count(1, 1))
                            for n in range(2):
                                if n:
                                    pe.wait_ge(q2_out, b.count(2, 1))
                                elif not first_batch(b):
                                    pe.wait_ge(x_added, b.count(1, X0 - 1))
                                for i in range(4):
                                    last = nc.tensor.matmul(small[:, i * S:(i + 1) * S],
                                                            mparts[:, 4 * n + i].rearrange("p e r -> p (e r)"),
                                                            ident_r[0:S, 0:S], start=True, stop=True)
                                last.then_inc(m_ps, 1)

                        def scores(b, g):
                            if g == 0:
                                pe.wait_ge(q2_out, b.count(2, 2))
                            for kc in range(KC):
                                i = g * KC + kc
                                pe.wait_ge(e_out, b.count(GROUPS * KC, E0 + i - 1))
                                ks = slice(kc * KP, (kc + 1) * KP)
                                bank = s2[i % 2]
                                if mask is not None:
                                    for part in range(2):
                                        nc.tensor.matmul(bank[0:KP, 0:4 * S], mask_r[:, part, ks], ident_r[0:S, :],
                                                         start=part == 0, stop=False)
                                for n in range(4):
                                    t, hi = head_of(g, n)
                                    rows = slice(64 * hi, 64 * hi + NSM)
                                    last = nc.tensor.matmul(bank[0:KP, n * S:(n + 1) * S], kst[rows, b.parity, t, ks],
                                                            q2[rows, t], start=mask is None, stop=mask is None or n == 3)
                                last.then_inc(s2_ps, 1)

                        def values(b, g):
                            if g == 0:
                                pe.wait_ge(o_out, b.count(1, O0))
                            pe.wait_ge(e_out, b.count(GROUPS * KC, E0 + (g + 1) * KC))
                            for kc in range(KC):
                                for n in range(4):
                                    t, hi = head_of(g, n)
                                    last = nc.tensor.matmul(av[32 * n:32 * n + 32, g * S:(g + 1) * S],
                                                            vx[:, b.parity, kc, 2 * t + hi],
                                                            es[:, g % 2, kc, n * S:(n + 1) * S], start=kc == 0,
                                                            stop=kc == KC - 1, tile_position=(0, 32 * n))
                            last.then_inc(av_ps, 1)

                        def output(b, ahead):
                            if ahead:
                                pe.wait_ge(q2_out, b.plus(1).count(2, 2))
                            else:
                                pe.wait_ge(x_added, b.count(1, X0))
                            pe.wait_ge(avs_out, b.count(1, 1))
                            for g in range(GROUPS):
                                last = nc.tensor.transpose(small[0:S, g * 128:(g + 1) * 128],
                                                           avs[:, g * S:(g + 1) * S], ident[:])
                            last.then_inc(avt_ps, 1)
                            pe.wait_ge(o_out, b.count(1, O0 + 1))
                            for c in range(DC):
                                last = nc.tensor.transpose(small[:, c * S:(c + 1) * S],
                                                           o_sb[:, c * 8:(c + 1) * 8, :].rearrange("p h d -> p (h d)"),
                                                           ident[0:S, 0:S])
                            last.then_inc(ot_ps, 1)
                            pe.wait_ge(ot_lo, b.count(1, 1))
                            if bias_out is not None:
                                nc.tensor.matmul(small[0:S, 0:D], ones[0:1, 0:S], bo[:], start=True, stop=False)
                            product3(nc, small[0:S, 0:D],
                                     [(ot[:, 0, k], ot[:, 1, k]) for k in range(DC)],
                                     [(wr_attn[:, 0, 3, k], wr_attn[:, 1, 3, k]) for k in range(DC)],
                                     first=bias_out is None).then_inc(y_ps, 1)

                        pe.wait_ge(filled, n_fill)
                        pe.wait_ge(const_in, n_const)
                        if mask is not None:
                            pe.wait_ge(mask_parts, 2)
                        for _ in range(AV0):
                            nc.tensor.matmul(av[0:2, 0:2], ident[:, 0:2], ident[:, 0:2], start=True, stop=True)\
                                .then_inc(av_ps, 1)
                        prepare(Batch(0, 0))
                        prepare(Batch(0, 1))
                        for g in range(GROUPS):
                            scores_for_max(Batch(0, 0), g)
                        max_rows(Batch(0, 0))

                        def turn(b, ahead):
                            for g in range(GROUPS):
                                scores(b, g)
                                if g:
                                    values(b, g - 1)
                                if ahead >= 1:
                                    scores_for_max(b.plus(1), g)
                            values(b, GROUPS - 1)
                            if ahead >= 1:
                                max_rows(b.plus(1))
                            output(b, ahead)
                            if ahead >= 2:
                                prepare(b.plus(2))

                        with pe.Fori(0, B // 2 - 1) as pair:
                            for parity in range(2):
                                turn(Batch(pair, parity), 2)
                        turn(Batch(B // 2 - 1, 0), 1)
                        turn(Batch(B // 2 - 1, 1), 0)
            end_phase()

        def experts_phase():
            st = ExitStack()
            scope.append(st)
            with st:
                squares = sb("ex_squares", [128, B * D])
                ysq = squares[:, 0:DC * T].rearrange("p (c t) -> p c t", c=DC)
                tick = sb("ex_tick", [1, 4])
                wp_sb = sb("wp_sb", [128, DC, D])
                bp_sb = sb("bp_sb", [128, DC])
                cen = sb("cen", [E, D])
                cen_sq = sb("cen_sq", [E, D])
                cen_s = sb("cen_s", [E, 4])
                cen_t = sb("cen_t", [128, DC, E])
                cen_t2 = sb("cen_t2", [128, DC, E])
                b1_nat = sb("b1_nat", [E * FC, 128])
                b1_t = sb("b1_t", [128, E, FC])
                b1_e = sb("b1_e", [128, 2, FC])
                b2_sb = sb("b2_sb", [E, D])
                yt = sb("yt", [128, DC, T])
                comb = sb("comb", [S, B, E])
                comb_t = sb("comb_t", [E, B, S])
                r1 = {n: sb(f"rt_{n}", [S, B]) for n in ("norm", "root", "sc", "xs", "om", "m1", "m2", "i1", "z")}
                r2 = {n: sb(f"rt_{n}", [S, B, E]) for n in ("a", "den", "eq", "oh1", "oh2", "iota")}
                pair2 = sb("rt_pair", [S, 2, B])
                prod2 = sb("rt_prod", [S, 2, B])
                root2 = sb("rt_root2", [S, 2, B])
                cn = sb("rt_cn", [S, E])
                cn1 = sb("rt_cn1", [S, E])
                stage = sb("w_stage", [128, 2, 2048])
                w1p = sb("w1_parts", [128, 2, 2, DC, F], F32R)
                w2p = sb("w2_parts", [128, 2, 2, FC, D], F32R)
                hf = sb("h_full", [128, 2, HALF])
                hp = sb("h_parts", [128, 2, 2, FC, HALF], F32R)
                hb = [pb(f"ex_h{i}") for i in range(3)]
                yb = [pb(f"ex_y{i}") for i in range(2)]
                ra, rb, rc = pb("rt_bank_a"), pb("rt_bank_b"), pb("rt_bank_c")

                small_in = sem("ex_small_in")
                w_in = [sem(f"ex_w_in{i}") for i in range(2)]
                w_hi = [sem(f"ex_w_hi{i}") for i in range(2)]
                w_lo = [sem(f"ex_w_lo{i}") for i in range(2)]
                t_ps = sem("ex_t_ps")
                t_hi = sem("ex_t_hi")
                t_lo = sem("ex_t_lo")
                cen_ss = sem("cen_ss")
                cen_root = sem("cen_root")
                cen_done = sem("cen_done")
                cen_ps = sem("cen_ps")
                cen_out = sem("cen_out")
                cn_ps = sem("cn_ps")
                y_ps = sem("rt_y_ps")
                y_out = sem("rt_y_out")
                ysq_out = sem("rt_ysq_out")
                g_ps = sem("rt_g_ps")
                nsq_ready = sem("rt_nsq_ready")
                norm_ready = sem("rt_norm_ready")
                pair_ready = sem("rt_pair_ready")
                root2_ready = sem("rt_root2_ready")
                comb_ready = sem("rt_comb_ready")
                ct_ps = sem("rt_ct_ps")
                ct_out = sem("rt_ct_out")
                bb_ps = sem("rt_bb_ps")
                bb_out = sem("rt_bb_out")
                b1_out = sem("ex_b1_out")
                h_ps = sem("ex_h_ps")
                h_act = sem("ex_h_act")
                h_hi = sem("ex_h_hi")
                h_lo = sem("ex_h_lo")
                e_ps = sem("ex_y_ps")
                e_out = sem("ex_y_out")
                link_dve = chain("ex_dve_chain")
                ln_dve, ln_act, xn_ready = layer_norm("ex", squares[0:S, :].rearrange("p (b d) -> p b d", b=B))
                W = 2048

                class Unit:
                    def __init__(self, expert, half):
                        self.e, self.half = expert, half

                    def next(self):
                        return Unit(self.e.plus(1), 0) if self.half else Unit(self.e, 1)

                    def count(self, n, within):
                        return self.e.count(2 * n, self.half * n + within)

                    def first(self):
                        return isinstance(self.e.pair, int) and (self.e.pair, self.e.parity, self.half) == (0, 0, 0)

                def units(eng, prologue, step):
                    prologue(Unit(Batch(0, 0), 0))
                    with eng.Fori(0, E // 2 - 1) as pair:
                        for parity in range(2):
                            for half in range(2):
                                step(Unit(Batch(pair, parity), half), True, True)
                    for parity in range(2):
                        for half in range(2):
                            step(Unit(Batch(E // 2 - 1, parity), half), not (parity and half), not parity)

                with nc.Block() as block:
                    @block.sync
                    def _(sp):
                        n = 16
                        sp.dma_start(wp_sb[:], w_p.rearrange("(c p) n -> p c n", p=128)).then_inc(small_in, n)
                        sp.dma_start(bp_sb[:], b_p.rearrange("(c p) -> p c", p=128),
                                     allow_slow_non_contiguous=True).then_inc(small_in, n)
                        sp.dma_start(cen[:], centroids).then_inc(small_in, n)
                        sp.dma_start(b1_nat[:], b_1.rearrange("e (c p) -> (e c) p", p=128)).then_inc(small_in, n)
                        sp.dma_start(b2_sb[:], b_2).then_inc(small_in, n)

                        def load(at, which):
                            if which == 0:
                                src = w_1[bass.ds(at, 1)].rearrange("o (c p) f -> p (o c) f", p=128)
                                dst = stage[:, 0].rearrange("p (c f) -> p c f", c=DC)
                            else:
                                src = w_2[bass.ds(at, 1)].rearrange("o (c p) d -> p (o c) d", p=128)
                                dst = stage[:, 1].rearrange("p (c d) -> p c d", c=FC)
                            sp.dma_start(dst, src).then_inc(w_in[which], 16)
                        load(0, 0)
                        load(0, 1)
                        next_expert = sp.alloc_register("next_expert")
                        with sp.Fori(0, E - 1) as e:
                            sp.reg_mov(next_expert, e + 1)
                            ahead = sp.snap(next_expert, min_val=1, max_val=E - 1)
                            for which in range(2):
                                sp.wait_ge(w_lo[which], ahead)
                                load(ahead, which)

                    @block.gpsimd
                    def _(pool):
                        def lower(e, which):
                            parts = (w1p, w2p)[which][:, e.parity].rearrange("p t a b -> p t (a b)")
                            pool.wait_ge(w_hi[which], e.count(1, 1))
                            nc.gpsimd.tensor_tensor(parts[:, 1], stage[:, which], parts[:, 0].bitcast(F32),
                                                    ALU.subtract).then_inc(w_lo[which], 1)
                        with pool.Fori(0, E // 2) as pair:
                            for parity in range(2):
                                for which in range(2):
                                    lower(Batch(pair, parity), which)

                    @block.scalar
                    def _(act):
                        def upper(e, which):
                            parts = (w1p, w2p)[which][:, e.parity].rearrange("p t a b -> p t (a b)")
                            act.wait_ge(w_in[which], e.count(16, 16))
                            nc.scalar.activation(parts[:, 0], stage[:, which], ACT.Copy).then_inc(w_hi[which], 1)
                        act.wait_ge(small_in, 80)
                        nc.scalar.activation(cen_sq[:], cen[:], ACT.Square, accum_out=cen_s[:, 0:1]).then_inc(cen_ss, 1)
                        act.wait_ge(cen_ss, 1)
                        nc.scalar.activation(cen_s[:, 1:2], cen_s[:, 0:1], ACT.Sqrt).then_inc(cen_root, 1)
                        upper(Batch(0, 0), 0)
                        upper(Batch(0, 0), 1)
                        ln_act(act)
                        for n in range(4):
                            c, half = n // 2, n % 2
                            act.wait_ge(t_ps, n + 1)
                            nc.scalar.activation(xnt[:, 0, c, half * HALF:(half + 1) * HALF],
                                                 ((hb + yb)[n])[:, 0:HALF], ACT.Copy).then_inc(t_hi, 1)
                        for n in range(4):
                            m, half = n // 2, n % 2
                            act.wait_ge(y_ps, n + 1)
                            nc.scalar.activation(yt[:, m, half * HALF:(half + 1) * HALF], (hb + yb)[n][:, 0:HALF],
                                                 ACT.Identity, bias=bp_sb[:, m:m + 1]).then_inc(y_out, 1)
                        act.wait_ge(nsq_ready, 1)
                        nc.scalar.activation(r1["root"][:], r1["norm"][:], ACT.Sqrt).then_inc(norm_ready, 1)
                        act.wait_ge(pair_ready, 1)
                        nc.scalar.activation(root2[:], prod2[:], ACT.Sqrt).then_inc(root2_ready, 1)

                        def gelus(u):
                            act.wait_ge(b1_out, u.e.count(1, 2))
                            for f in range(FC):
                                act.wait_ge(h_ps, u.count(FC, f + 1))
                                if f >= 2 or not u.first():
                                    act.wait_ge(h_lo, u.count(FC, f - 1))
                                nc.scalar.activation(hf[:, f % 2], hb[f % 2][:, 0:HALF], ACT.Gelu,
                                                     bias=b1_e[:, u.e.parity, f:f + 1]).then_inc(h_act, 1)

                        def step(u, more, split):
                            if split and u.half == 0:
                                act.wait_ge(h_ps, u.count(FC, FC))
                                upper(u.e.plus(1), 0)
                            if more:
                                gelus(u.next())
                            if split and u.half == 0:
                                act.wait_ge(e_ps, u.count(4, Y0))
                                upper(u.e.plus(1), 1)
                        units(act, gelus, step)

                    @block.vector
                    def _(dve):
                        link = link_dve(dve)
                        for e in range(E):
                            nc.vector.memset(r2["iota"][:, :, e], float(e)).then_inc(cen_done, 1)
                        dve.wait_ge(cen_done, E)
                        dve.wait_ge(cen_root, 1)
                        link(nc.vector.tensor_scalar(cen_s[:, 2:3], cen_s[:, 1:2], 1e-7, None, ALU.max))
                        link(nc.vector.reciprocal(cen_s[:, 3:4], cen_s[:, 2:3]))
                        link(nc.vector.tensor_scalar(cen_s[:, 2:3], cen_s[:, 3:4], 0.95, 1.0, ALU.mult, ALU.min))
                        nc.vector.tensor_scalar(cen_sq[:], cen[:], cen_s[:, 2:3], None, ALU.mult).then_inc(cen_done, 1)
                        dve.wait_ge(cen_ps, 1)
                        link(nc.vector.tensor_copy(cen_t[:].rearrange("p c e -> p (c e)"), rc[:, 0:DC * E]))
                        link(nc.vector.tensor_copy(b1_t[:].rearrange("p e c -> p (e c)"), rc[:, 64:64 + E * FC]))
                        nc.vector.tensor_tensor(cen_t2[:], cen_t[:], cen_t[:], ALU.mult).then_inc(cen_out, 1)
                        ln_dve(dve, link)
                        for n in range(4):
                            c, half = n // 2, n % 2
                            cols = slice(half * HALF, (half + 1) * HALF)
                            dve.wait_ge(t_hi, n + 1)
                            nc.vector.tensor_tensor(xnt[:, 1, c, cols], (hb + yb)[n][:, 0:HALF],
                                                    xnt[:, 0, c, cols].bitcast(F32), ALU.subtract).then_inc(t_lo, 1)
                        dve.wait_ge(cn_ps, 1)
                        link(nc.vector.tensor_scalar(cn[:], rb[0:S, 0:E], 0.99, None, ALU.min))
                        link(nc.vector.tensor_scalar(cn1[:], cn[:], -1.0, 1.0, ALU.mult, ALU.add))
                        dve.wait_ge(y_out, 4)
                        for m in range(DC):
                            nc.vector.tensor_tensor(ysq[:, m], yt[:, m], yt[:, m], ALU.mult).then_inc(ysq_out, 1)
                        dve.wait_ge(g_ps, 1)
                        g = ra[0:S, 0:16 * B].rearrange("p (b k) -> p b k", b=B)
                        nc.vector.tensor_copy(r1["norm"][:], g[:, :, E]).then_inc(nsq_ready, 1)
                        dve.wait_ge(norm_ready, 1)

                        def wide(a):
                            return a.rearrange("p (b o) -> p b o", o=1).broadcast_to([S, B, E])

                        def over(a):
                            return a.rearrange("p (o e) -> p o e", o=1).broadcast_to([S, B, E])
                        v = nc.vector
                        link(v.tensor_scalar(r1["z"][:], r1["root"][:], 1e-7, None, ALU.max))
                        link(v.reciprocal(r1["m1"][:], r1["z"][:]))
                        link(v.tensor_scalar(r1["sc"][:], r1["m1"][:], 0.95, 1.0, ALU.mult, ALU.min))
                        link(v.tensor_tensor(r1["m2"][:], r1["sc"][:], r1["sc"][:], ALU.mult))
                        link(v.tensor_tensor(r1["xs"][:], r1["m2"][:], r1["norm"][:], ALU.mult))
                        link(v.tensor_scalar(r1["xs"][:], r1["xs"][:], 0.99, None, ALU.min))
                        link(v.tensor_scalar(r1["om"][:], r1["xs"][:], -1.0, 1.0, ALU.mult, ALU.add))
                        a, den, eq, oh1, oh2, iota = (r2[n] for n in ("a", "den", "eq", "oh1", "oh2", "iota"))
                        link(v.tensor_tensor(a[:], g[:, :, 0:E], wide(r1["sc"][:]), ALU.mult))
                        link(v.tensor_tensor(den[:], wide(r1["xs"][:]), over(cn[:]), ALU.add))
                        link(v.scalar_tensor_tensor(a[:], a[:], -2.0, den[:], ALU.mult, ALU.add))
                        link(v.tensor_scalar(a[:], a[:], 0.0, 2.0, ALU.max, ALU.mult))
                        link(v.tensor_tensor(den[:], wide(r1["om"][:]), over(cn1[:]), ALU.mult))
                        link(v.tensor_scalar(den[:], den[:], 1e-7, None, ALU.add))
                        link(v.reciprocal(eq[:], den[:]))
                        link(v.tensor_tensor(a[:], a[:], eq[:], ALU.mult))
                        link(v.tensor_scalar(a[:], a[:], 1.0, 1.0 + 2.0 ** -23, ALU.add, ALU.max))

                        def nearest(m, onehot):
                            link(v.tensor_reduce(m, a[:], AX.X, ALU.min))
                            link(v.tensor_tensor(eq[:], a[:], wide(m), ALU.not_equal))
                            link(v.scalar_tensor_tensor(eq[:], eq[:], 100.0, iota[:], ALU.mult, ALU.add))
                            link(v.tensor_reduce(r1["i1"][:], eq[:], AX.X, ALU.min))
                            link(v.tensor_tensor(onehot[:], iota[:], wide(r1["i1"][:]), ALU.is_equal))
                        nearest(pair2[:, 0], oh1)
                        link(v.scalar_tensor_tensor(a[:], oh1[:], 1e30, a[:], ALU.mult, ALU.add))
                        nearest(pair2[:, 1], oh2)
                        link(v.tensor_scalar(prod2[:], pair2[:], 1.0, None, ALU.add))
                        link(v.tensor_scalar(root2[:], pair2[:], -1.0, None, ALU.add))
                        v.tensor_tensor(prod2[:], prod2[:], root2[:], ALU.mult).then_inc(pair_ready, 1)
                        dve.wait_ge(root2_ready, 1)
                        link(v.tensor_tensor(pair2[:], pair2[:], root2[:], ALU.add))
                        link(v.tensor_tensor(r1["z"][:], pair2[:, 0], pair2[:, 1], ALU.add))
                        link(v.reciprocal(r1["m1"][:], r1["z"][:]))
                        link(v.tensor_tensor(r1["m2"][:], pair2[:, 1], r1["m1"][:], ALU.mult))
                        link(v.tensor_tensor(r1["z"][:], pair2[:, 0], r1["m1"][:], ALU.mult))
                        link(v.tensor_tensor(oh1[:], oh1[:], wide(r1["m2"][:]), ALU.mult))
                        link(v.tensor_tensor(oh2[:], oh2[:], wide(r1["z"][:]), ALU.mult))
                        v.tensor_tensor(comb[:], oh1[:], oh2[:], ALU.add).then_inc(comb_ready, 1)
                        for n in range(2):
                            dve.wait_ge(ct_ps, n + 1)
                            v.tensor_copy(comb_t[:, 4 * n:4 * n + 4, :].rearrange("p b s -> p (b s)"),
                                          (ra, rb)[n][0:E, 0:4 * S]).then_inc(ct_out, 1)
                        for n in range(4):
                            dve.wait_ge(bb_ps, n + 1)
                            bank = (ra, rb)[n % 2]
                            rows = x_sb[:, 2 * n:2 * n + 2, :].rearrange("p b d -> p (b d)")
                            v.tensor_tensor(rows, rows, bank[0:S, :], ALU.add).then_inc(bb_out, 1)
                        v.memset(tick[:, 0:1], 0.0).then_inc(b1_out, 1)
                        for n in range(R0):
                            v.memset(tick[:, n + 1:n + 2], 0.0).then_inc(e_out, 1)
                        dve.wait_ge(bb_out, 4)
                        dve.wait_ge(b1_out, 1)

                        def split(u):
                            if u.half == 0:
                                v.tensor_scalar(b1_e[:, u.e.parity:u.e.parity + 1, :],
                                                b1_t[:, bass.ds(u.e.index(), 1), :], 1.0, None, ALU.mult)\
                                    .then_inc(b1_out, 1)
                            for f in range(FC):
                                dve.wait_ge(h_act, u.count(FC, f + 1))
                                v.tensor_copy(hp[:, u.half, 0, f], hf[:, f % 2]).then_inc(h_hi, 1)
                                dve.wait_ge(h_hi, u.count(FC, f + 1))
                                v.tensor_tensor(hp[:, u.half, 1, f], hf[:, f % 2], hp[:, u.half, 0, f].bitcast(F32),
                                                ALU.subtract).then_inc(h_lo, 1)

                        def step(u, more, _):
                            if more:
                                split(u.next())
                            for n in range(4):
                                t = 4 * u.half + n
                                dve.wait_ge(e_ps, u.count(4, Y0 + n + 1))
                                v.scalar_tensor_tensor(x_sb[:, t, :], yb[n % 2][0:S, 0:D],
                                                       comb[:, t, bass.ds(u.e.index(), 1)], x_sb[:, t, :],
                                                       ALU.mult, ALU.add).then_inc(e_out, 1)
                        units(dve, split, step)

                    @block.tensor
                    def _(pe):
                        pe.wait_ge(small_in, 80)
                        pe.wait_ge(cen_done, E + 1)
                        for c in range(DC):
                            nc.tensor.transpose(rc[:, c * E:(c + 1) * E], cen_sq[:, c * 128:(c + 1) * 128],
                                                ident[0:E, 0:E])
                        nc.tensor.transpose(rc[:, 64:64 + E * FC], b1_nat[:], ident[0:E * FC, 0:E * FC])\
                            .then_inc(cen_ps, 1)
                        pe.wait_ge(cen_out, 1)
                        for c in range(DC):
                            last = nc.tensor.matmul(rb[0:S, 0:E], ones[:, 0:S], cen_t2[:, c], start=c == 0, stop=c == 1)
                        last.then_inc(cn_ps, 1)
                        pe.wait_ge(xn_ready, 1)
                        for n in range(4):
                            c, half = n // 2, n % 2
                            for b in range(4):
                                last = nc.tensor.transpose((hb + yb)[n][:, b * S:(b + 1) * S],
                                                           xn[:, 4 * half + b, c * 128:(c + 1) * 128],
                                                           ident[0:S, 0:S])
                            last.then_inc(t_ps, 1)
                        pe.wait_ge(t_lo, 4)
                        for n in range(4):
                            m, half = n // 2, n % 2
                            cols = slice(half * HALF, (half + 1) * HALF)
                            i = 0
                            for k in range(DC):
                                for part in range(2):
                                    last = nc.tensor.matmul((hb + yb)[n][:, 0:HALF], wp_sb[:, k, m * 128:(m + 1) * 128],
                                                            xnt[:, part, k, cols].bitcast(F32),
                                                            start=i == 0, stop=i == 3)
                                    i += 1
                            last.then_inc(y_ps, 1)
                        pe.wait_ge(y_out, 4)
                        pe.wait_ge(ysq_out, DC)
                        for b in range(B):
                            cols = slice(b * S, (b + 1) * S)
                            for k in range(DC):
                                nc.tensor.matmul(ra[0:S, 16 * b:16 * b + E], yt[:, k, cols], cen_t[:, k],
                                                 start=k == 0, stop=k == 1)
                            for k in range(DC):
                                last = nc.tensor.matmul(ra[0:S, 16 * b + E:16 * b + E + 1], ysq[:, k, cols],
                                                        ones[:, 0:1], start=k == 0, stop=k == 1)
                        last.then_inc(g_ps, 1)

                        def up(u):
                            if u.half == 0:
                                pe.wait_ge(w_lo[0], u.e.count(1, 1))
                            cols = slice(u.half * HALF, (u.half + 1) * HALF)
                            for f in range(FC):
                                if f >= 2 or not u.first():
                                    pe.wait_ge(h_act, u.count(FC, f - 1))
                                fs = slice(f * 128, (f + 1) * 128)
                                w = w1p[:, u.e.parity]
                                product3(nc, hb[f % 2][:, 0:HALF],
                                         [(w[:, 0, k, fs], w[:, 1, k, fs]) for k in range(DC)],
                                         [(xnt[:, 0, k, cols], xnt[:, 1, k, cols]) for k in range(DC)])\
                                    .then_inc(h_ps, 1)

                        def down(u):
                            if u.half == 0:
                                pe.wait_ge(w_lo[1], u.e.count(1, 1))
                            pe.wait_ge(h_lo, u.count(FC, FC))
                            for n in range(4):
                                pe.wait_ge(e_out, u.count(4, R0 + n - 1))
                                ts = slice(n * S, (n + 1) * S)
                                product3(nc, yb[n % 2][0:S, 0:D],
                                         [(hp[:, u.half, 0, f, ts], hp[:, u.half, 1, f, ts]) for f in range(FC)],
                                         [(w2p[:, u.e.parity, 0, f], w2p[:, u.e.parity, 1, f]) for f in range(FC)])\
                                    .then_inc(e_ps, 1)

                        def step(u, more, _):
                            if more:
                                up(u.next())
                            down(u)

                        def start(u):
                            pe.wait_ge(comb_ready, 1)
                            for n in range(2):
                                for b in range(4):
                                    last = nc.tensor.transpose((ra, rb)[n][0:E, b * S:(b + 1) * S],
                                                               comb[:, 4 * n + b, :], ident[0:S, 0:S])
                                last.then_inc(ct_ps, 1)
                            pe.wait_ge(ct_out, 2)
                            for n in range(4):
                                if n >= 2:
                                    pe.wait_ge(bb_out, n - 1)
                                for b in range(2):
                                    last = nc.tensor.matmul((ra, rb)[n % 2][0:S, b * D:(b + 1) * D],
                                                            comb_t[:, 2 * n + b, :], b2_sb[:], start=True, stop=True)
                                last.then_inc(bb_ps, 1)
                            for n in range(Y0):
                                nc.tensor.matmul(rc[0:2, 0:2], ident[:, 0:2], ident[:, 0:2], start=True,
                                                 stop=True).then_inc(e_ps, 1)
                            up(u)
                        units(pe, start, step)
            end_phase()

        def bit_ffn_phase():
            st = ExitStack()
            scope.append(st)
            with st:
                NR = 2.0 ** 23 * 1.5
                squares = sb("bf_squares", [128, B * D])
                wu = sb("wu", [128, FC, D])
                wd = sb("wd", [128, DC, F])
                wu_q = sb("wu_q", [128, FC, D], BF16)
                wd_q = sb("wd_q", [128, DC, F], BF16)
                wu_t = sb("wu_t", [128, DC, F], BF16)
                wd_t = sb("wd_t", [128, FC, D], BF16)
                ident_b = sb("ident_b", [128, 128], BF16)
                wsum = sb("wsum", [128, 2])
                wmean = sb("wmean", [128, 2])
                wrec = sb("wrec", [128, 2])
                cw = sb("cw", [128, FC, 3])
                cb = sb("cb", [128, FC])
                am = sb("bf_am", [S, B])
                rs = sb("bf_rs", [S, B])
                dq = sb("bf_dq", [S, B])
                dq2 = sb("bf_dq2", [S, B])
                xq = sb("bf_xq", [S, B, D], BF16)
                xq_t = sb("bf_xqt", [128, DC, T], BF16)
                diag = sb("bf_diag", [S, 2, B, S])
                row1 = sb("bf_row1", [128, T])
                row2 = sb("bf_row2", [128, T])
                hpad = sb("bf_hpad", [128, 2, B, S + 2])
                conv = sb("bf_conv", [128, 2, B, S])
                hs = sb("bf_hs", [128, FC, T])
                hq = sb("bf_hq", [128, FC, T], BF16)
                amx = sb("bf_amx", [128, T])
                tick = sb("bf_tick", [1, 1])
                pu = [pb(f"bf_u{i}") for i in range(4)]
                pt = [pb(f"bf_t{i}", (128, 1024), BF16) for i in range(2)]
                pr = [pb(f"bf_r{i}") for i in range(2)]

                w_in = sem("bf_w_in")
                c_in = sem("bf_c_in")
                idb = sem("bf_idb")
                ws_out = sem("bf_ws_out")
                ws_ps = sem("bf_ws_ps")
                wq_out = sem("bf_wq_out")
                wt_ps = sem("bf_wt_ps")
                wt_out = sem("bf_wt_out")
                xq_out = sem("bf_xq_out")
                xt_ps = sem("bf_xt_ps")
                xt_out = sem("bf_xt_out")
                dg = sem("bf_dg")
                row_ps = sem("bf_row_ps")
                row_out = sem("bf_row_out")
                u_ps = sem("bf_u_ps")
                u_out = sem("bf_u_out")
                c_mid = sem("bf_c_mid")
                c_left = sem("bf_c_left")
                c_right = sem("bf_c_right")
                s_out = sem("bf_s_out")
                m_out = sem("bf_m_out")
                am_ps = sem("bf_am_ps")
                hq_out = sem("bf_hq_out")
                d_ps = sem("bf_d_ps")
                d_out = sem("bf_d_out")
                link_dve = chain("bf_dve_chain")
                ln_dve, ln_act, xn_ready = layer_norm("bf", squares[0:S, :].rearrange("p (b d) -> p b d", b=B))

                def wide(a, n):
                    return a.rearrange("p (b o) -> p b o", o=1).broadcast_to([S, B, n])

                with nc.Block() as block:
                    @block.sync
                    def _(sp):
                        sp.dma_start(wu[:], w_up.rearrange("(c p) k -> p c k", p=128)).then_inc(w_in, 16)
                        sp.dma_start(wd[:], w_down.rearrange("(c p) k -> p c k", p=128)).then_inc(w_in, 16)
                        sp.dma_start(cw[:], conv_w.rearrange("(c p) o k -> p c (o k)", p=128)).then_inc(c_in, 16)
                        sp.dma_start(cb[:], conv_b.rearrange("(c p) -> p c", p=128),
                                     allow_slow_non_contiguous=True).then_inc(c_in, 16)

                    @block.scalar
                    def _(act):
                        ln_act(act)
                        for n in range(4):
                            act.wait_ge(wt_ps, n + 1)
                            dst = wu_t[:, n] if n < 2 else wd_t[:, 4 * (n - 2):4 * (n - 1)].rearrange("p c d -> p (c d)")
                            nc.scalar.activation(dst, pt[n % 2][:], ACT.Copy).then_inc(wt_out, 1)
                        for n in range(2):
                            act.wait_ge(row_ps, 2 * n + 2)
                            for half in range(2):
                                nc.scalar.activation((row1, row2)[n][:, half * HALF:(half + 1) * HALF],
                                                     pr[half][:, 0:HALF], ACT.Copy).then_inc(row_out, 1)
                            if n:
                                break
                            act.wait_ge(c_in, 32)
                            for j in range(FC):
                                act.wait_ge(u_out, 2 * j + 2)
                                if j >= 2:
                                    act.wait_ge(s_out, j - 1)
                                nc.scalar.activation(conv[:, j % 2], hpad[:, j % 2, :, 1:S + 1], ACT.Identity,
                                                     bias=cb[:, j:j + 1], scale=cw[:, j, 1:2]).then_inc(c_mid, 1)
                                act.wait_ge(c_right, j + 1)
                                nc.scalar.activation(hs[:, j], conv[:, j % 2].rearrange("p b s -> p (b s)"),
                                                     ACT.Silu).then_inc(s_out, 1)

                    @block.vector
                    def _(dve):
                        link = link_dve(dve)
                        v = nc.vector
                        link(v.tensor_copy(ident_b[:], ident[:]))
                        link(v.memset(hpad[:], 0.0))
                        link(v.memset(amx[:], 0.0))
                        v.memset(diag[:], 0.0).then_inc(idb, 1)
                        dve.wait_ge(w_in, 32)
                        for n, w in enumerate((wu, wd)):
                            v.tensor_reduce(wsum[:, n:n + 1], w[:].rearrange("p a b -> p (a b)"), AX.X, ALU.add,
                                            apply_absolute_value=True).then_inc(ws_out, 1)
                        dve.wait_ge(ws_ps, 1)
                        link(v.tensor_scalar(wmean[:], pr[0][:, 0:2], 1.0 / (D * F), 1e-5, ALU.mult, ALU.max))
                        link(v.reciprocal(wrec[:], wmean[:]))
                        for n, (w, q) in enumerate(((wu, wu_q), (wd, wd_q))):
                            flat = w[:].rearrange("p a b -> p (a b)")
                            link(v.tensor_scalar(flat, flat, wrec[:, n:n + 1], NR, ALU.mult, ALU.add))
                            link(v.tensor_scalar(flat, flat, NR, -1.0, ALU.subtract, ALU.max))
                            v.tensor_scalar(q[:].rearrange("p a b -> p (a b)"), flat, 1.0, None, ALU.min)\
                                .then_inc(wq_out, 1)
                        ln_dve(dve, link)
                        dve.wait_ge(xn_ready, 1)
                        link(v.tensor_reduce(am[:], xn[:], AX.X, ALU.max, apply_absolute_value=True))
                        link(v.tensor_scalar(am[:], am[:], 1e-5, None, ALU.max))
                        link(v.reciprocal(rs[:], am[:]))
                        link(v.tensor_scalar(rs[:], rs[:], 127.0, None, ALU.mult))
                        link(v.tensor_scalar(dq[:], am[:], 1.0 / 127.0, None, ALU.mult))
                        link(v.tensor_scalar(dq[:], dq[:], wmean[0:S, 0:1], None, ALU.mult))
                        link(v.tensor_tensor(xn[:], xn[:], wide(rs[:], D), ALU.mult))
                        link(v.tensor_scalar(xn[:], xn[:], NR, NR, ALU.add, ALU.subtract))
                        v.tensor_scalar(xq[:], xn[:], -128.0, 127.0, ALU.max, ALU.min).then_inc(xq_out, 1)
                        for b in range(B):
                            v.tensor_scalar(diag[:, 0, b], ident[0:S, 0:S], dq[:, b:b + 1], None, ALU.mult)\
                                .then_inc(dg, 1)
                        for n in range(2):
                            dve.wait_ge(xt_ps, n + 1)
                            v.tensor_copy(xq_t[:, n], pt[n][:, 0:T]).then_inc(xt_out, 1)
                        dve.wait_ge(row_out, 2)
                        dve.wait_ge(c_in, 32)

                        for j in range(FC + 1):
                            if j < FC:
                                if j >= 2:
                                    dve.wait_ge(c_right, j - 1)
                                    dve.wait_ge(c_mid, j - 1)
                                for half in range(2):
                                    dve.wait_ge(u_ps, 2 * j + half + 1)
                                    cols = slice(half * HALF, (half + 1) * HALF)
                                    v.tensor_tensor(hpad[:, j % 2, 4 * half:4 * half + 4, 1:S + 1],
                                                    pu[(2 * j + half) % 4][:, 0:HALF].rearrange("p (b s) -> p b s", b=4),
                                                    row1[:, cols].rearrange("p (b s) -> p b s", b=4),
                                                    ALU.mult).then_inc(u_out, 1)
                            if j:
                                i = j - 1
                                dve.wait_ge(c_mid, i + 1)
                                v.scalar_tensor_tensor(conv[:, i % 2], hpad[:, i % 2, :, 0:S], cw[:, i, 0:1],
                                                       conv[:, i % 2], ALU.mult, ALU.add).then_inc(c_left, 1)
                                dve.wait_ge(c_left, i + 1)
                                v.scalar_tensor_tensor(conv[:, i % 2], hpad[:, i % 2, :, 2:S + 2], cw[:, i, 2:3],
                                                       conv[:, i % 2], ALU.mult, ALU.add).then_inc(c_right, 1)
                                for k in ([i - 1] if i else []) + ([i] if i == FC - 1 else []):
                                    dve.wait_ge(s_out, k + 1)
                                    link(v.tensor_tensor(amx[:], amx[:], hs[:, k], ALU.max))
                                    link(v.scalar_tensor_tensor(amx[:], hs[:, k], -1.0, amx[:], ALU.mult, ALU.max))
                        v.tensor_copy(tick[:], amx[0:1, 0:1]).then_inc(m_out, 1)
                        dve.wait_ge(am_ps, 2)
                        for half in range(2):
                            link(v.tensor_reduce(am[:, 4 * half:4 * half + 4],
                                                 pu[half][0:S, :].rearrange("p (b c) -> p b c", b=4), AX.X, ALU.max,
                                                 apply_absolute_value=True))
                        link(v.tensor_scalar(am[:], am[:], 1e-5, None, ALU.max))
                        link(v.reciprocal(rs[:], am[:]))
                        link(v.tensor_scalar(rs[:], rs[:], 127.0, None, ALU.mult))
                        link(v.tensor_scalar(dq2[:], am[:], 1.0 / 127.0, None, ALU.mult))
                        link(v.tensor_scalar(dq2[:], dq2[:], wmean[0:S, 1:2], None, ALU.mult))
                        for b in range(B):
                            v.tensor_scalar(diag[:, 1, b], ident[0:S, 0:S], rs[:, b:b + 1], None, ALU.mult)\
                                .then_inc(dg, 1)
                        dve.wait_ge(row_out, 4)
                        for j in range(FC):
                            link(v.tensor_tensor(hs[:, j], hs[:, j], row2[:], ALU.mult))
                            link(v.tensor_scalar(hs[:, j], hs[:, j], NR, NR, ALU.add, ALU.subtract))
                            v.tensor_scalar(hq[:, j], hs[:, j], -128.0, 127.0, ALU.max, ALU.min).then_inc(hq_out, 1)
                        for b in range(B):
                            dve.wait_ge(d_ps, b + 1)
                            v.scalar_tensor_tensor(x_sb[:, b, :], pu[b % 4][0:S, 0:D], dq2[:, b:b + 1], x_sb[:, b, :],
                                                   ALU.mult, ALU.add).then_inc(d_out, 1)

                    @block.tensor
                    def _(pe):
                        pe.wait_ge(ws_out, 2)
                        nc.tensor.matmul(pr[0][:, 0:2], ones[:], wsum[:], start=True, stop=True).then_inc(ws_ps, 1)
                        pe.wait_ge(idb, 1)
                        for n in range(4):
                            pe.wait_ge(wq_out, 1 if n < 2 else 2)
                            if n >= 2:
                                pe.wait_ge(wt_out, n - 1)
                            for i in range(8):
                                if n < 2:
                                    last = nc.tensor.transpose(pt[n % 2][:, i * 128:(i + 1) * 128],
                                                               wu_q[:, i, n * 128:(n + 1) * 128], ident_b[:])
                                else:
                                    c, o = 4 * (n - 2) + i // 2, i % 2
                                    last = nc.tensor.transpose(pt[n % 2][:, i * 128:(i + 1) * 128],
                                                               wd_q[:, o, c * 128:(c + 1) * 128], ident_b[:])
                            last.then_inc(wt_ps, 1)
                        pe.wait_ge(xq_out, 1)
                        pe.wait_ge(wt_out, 4)
                        for n in range(2):
                            for b in range(B):
                                last = nc.tensor.transpose(pt[n][:, b * S:(b + 1) * S], xq[:, b, n * 128:(n + 1) * 128],
                                                           ident_b[0:S, 0:S])
                            last.then_inc(xt_ps, 1)

                        def spread(which):
                            pe.wait_ge(dg, B * (which + 1))
                            if which:
                                pe.wait_ge(row_out, 2)
                            for half in range(2):
                                nc.tensor.matmul(pr[half][:, 0:HALF], ones[0:S, :],
                                                 diag[:, which, 4 * half:4 * half + 4].rearrange("p b s -> p (b s)"),
                                                 start=True, stop=True).then_inc(row_ps, 1)
                        spread(0)
                        pe.wait_ge(xt_out, 2)
                        for j in range(FC):
                            for half in range(2):
                                n = 2 * j + half
                                if n >= 4:
                                    pe.wait_ge(u_out, n - 3)
                                for k in range(DC):
                                    last = nc.tensor.matmul(pu[n % 4][:, 0:HALF], wu_t[:, k, j * 128:(j + 1) * 128],
                                                            xq_t[:, k, half * HALF:(half + 1) * HALF],
                                                            start=k == 0, stop=k == 1)
                                last.then_inc(u_ps, 1)
                        pe.wait_ge(u_out, 2 * FC)
                        pe.wait_ge(m_out, 1)
                        for half in range(2):
                            for i in range(4):
                                b = 4 * half + i
                                last = nc.tensor.transpose(pu[half][0:S, i * 128:(i + 1) * 128],
                                                           amx[:, b * S:(b + 1) * S], ident[:])
                            last.then_inc(am_ps, 1)
                        spread(1)
                        pe.wait_ge(hq_out, FC)
                        for b in range(B):
                            if b >= 4:
                                pe.wait_ge(d_out, b - 3)
                            for j in range(FC):
                                last = nc.tensor.matmul(pu[b % 4][0:S, 0:D], hq[:, j, b * S:(b + 1) * S], wd_t[:, j],
                                                        start=j == 0, stop=j == FC - 1)
                            last.then_inc(d_ps, 1)
            end_phase()

        rows = "(c p) n -> p c n"
        for layer in range(2):
            st = ExitStack()
            scope.append(st)
            with st:
                w_attn = sb(f"w_attn{layer}", [128, 4, DC, D])
                wr_attn = sb(f"wr_attn{layer}", [128, 2, 4, DC, D], F32R)
                if layer == 0:
                    sources = (w_q0, w_kv0[:, 0:D], w_kv0[:, D:2 * D], w_out0)
                    queries("q0", [(n, w.rearrange(rows, p=128)) for n, w in enumerate(sources)], False, b_q0)
                    attention("a0", DH ** -0.5, b_kv0, b_out0, None)
                else:
                    sources = (w_q1, w_kv1[0:D], w_kv1[D:2 * D], w_out1)
                    queries("q1", [(n, w.rearrange(rows, p=128)) for n, w in enumerate(sources)], True, None)
                    attention("a1", D ** -0.5, None, None, mask)
            end_phase()
            if layer == 0:
                experts_phase()
        bit_ffn_phase()
        fin = ExitStack()
        scope.append(fin)
        with fin:
            stored = sem("stored")
            with nc.Block() as block:
                @block.sync
                def _(sp):
                    sp.dma_start(out.rearrange("b s d -> s b d"), x_sb[:]).then_inc(stored, 16)
                    sp.wait_ge(stored, 16)
        end_phase()


_INS = ["x", "ctx_1024", "mask_SxS2_fk0", "L0_xattn_w_q", "L0_xattn_b_q", "L0_xattn_w_kv", "L0_xattn_b_kv",
        "L0_xattn_w_out", "L0_xattn_b_out", "L0_ffn_centroids", "L0_ffn_Wp", "L0_ffn_bp", "L0_ffn_W1", "L0_ffn_b1",
        "L0_ffn_W2", "L0_ffn_b2", "L1_xattn_Wq", "L1_xattn_Wkv", "L1_xattn_Wout", "L1_ffn_w1", "L1_ffn_conv_w",
        "L1_ffn_conv_b", "L1_ffn_w2"]


def kernel(**inputs):
    import numpy as _np
    import concourse.bacc as _bacc
    from concourse import mybir as _mybir
    from concourse.bass_utils import run_bass_kernel_spmd as _run

    nc = _bacc.Bacc("TRN2", target_bir_lowering=False, num_devices=1)
    arrays, args = {}, []
    for name in _INS:
        a = _np.ascontiguousarray(inputs[name])
        arrays[f"in_{name}"] = a
        args.append(nc.dram_tensor(f"in_{name}", a.shape, _mybir.dt.from_np(a.dtype), kind="ExternalInput").ap())
    args.append(nc.dram_tensor("out_x", (B, S, D), _mybir.dt.float32, kind="ExternalOutput").ap())
    xattn_ffn_kernel(nc, *args)
    r = _run(nc, [arrays], core_ids=[0])
    return r.results[0]["out_x"]
```
